# Optimizing a Trainium2 kernel written in Bass

```python
import numpy as np
import jax
import jax.numpy as jnp

def _softmax(x, axis=-1):
    return jax.nn.softmax(x, axis=axis)

def _gelu(x):
    return jax.nn.gelu(x, approximate=True)

def _silu(x):
    return jax.nn.silu(x)

def _sigmoid(x):
    return jax.nn.sigmoid(x)

def _layernorm(x, axis=-1, eps=1e-05):
    m = jnp.mean(x, axis=axis, keepdims=True)
    v = jnp.var(x, axis=axis, keepdims=True)
    return (x - m) / jnp.sqrt(v + eps)

def _scatter_add(tgt, idx, src, axis=0):
    return tgt.at[idx].add(src)

def _segment_sum(src, seg, n):
    return jax.ops.segment_sum(src, seg, n)
kernel_name = 'mk_dlrm_tower_d1_rec_r8_d2c5d3'

def setup_inputs(seed: int=0):
    np.random.seed(seed)
    _w = jnp.asarray

    def _rec_inputs():
        import jax
        import jax.numpy as jnp
        _tk = jax.random.key(seed)
        ids = jnp.stack([jax.random.randint(jax.random.fold_in(_tk, 200 + f), (512,), 0, v, jnp.int32) for f, v in enumerate([1000, 1000, 1000, 1250, 1250, 125000, 1000, 1000, 1000, 12500, 1000, 1250, 1250, 12500, 12500, 1000, 12500, 12500, 12500, 12500, 1000, 1250, 12500, 1250, 1000, 1250])], axis=1)
        tbl_0 = 0.05 * jax.random.normal(jax.random.fold_in(_tk, 500 + 0), (1000, 128), jnp.float32)
        tbl_1 = 0.05 * jax.random.normal(jax.random.fold_in(_tk, 500 + 1), (1000, 128), jnp.float32)
        tbl_2 = 0.05 * jax.random.normal(jax.random.fold_in(_tk, 500 + 2), (1000, 128), jnp.float32)
        tbl_3 = 0.05 * jax.random.normal(jax.random.fold_in(_tk, 500 + 3), (1250, 128), jnp.float32)
        tbl_4 = 0.05 * jax.random.normal(jax.random.fold_in(_tk, 500 + 4), (1250, 128), jnp.float32)
        tbl_5 = 0.05 * jax.random.normal(jax.random.fold_in(_tk, 500 + 5), (125000, 128), jnp.float32)
        tbl_6 = 0.05 * jax.random.normal(jax.random.fold_in(_tk, 500 + 6), (1000, 128), jnp.float32)
        tbl_7 = 0.05 * jax.random.normal(jax.random.fold_in(_tk, 500 + 7), (1000, 128), jnp.float32)
        tbl_8 = 0.05 * jax.random.normal(jax.random.fold_in(_tk, 500 + 8), (1000, 128), jnp.float32)
        tbl_9 = 0.05 * jax.random.normal(jax.random.fold_in(_tk, 500 + 9), (12500, 128), jnp.float32)
        tbl_10 = 0.05 * jax.random.normal(jax.random.fold_in(_tk, 500 + 10), (1000, 128), jnp.float32)
        tbl_11 = 0.05 * jax.random.normal(jax.random.fold_in(_tk, 500 + 11), (1250, 128), jnp.float32)
        tbl_12 = 0.05 * jax.random.normal(jax.random.fold_in(_tk, 500 + 12), (1250, 128), jnp.float32)
        tbl_13 = 0.05 * jax.random.normal(jax.random.fold_in(_tk, 500 + 13), (12500, 128), jnp.float32)
        tbl_14 = 0.05 * jax.random.normal(jax.random.fold_in(_tk, 500 + 14), (12500, 128), jnp.float32)
        tbl_15 = 0.05 * jax.random.normal(jax.random.fold_in(_tk, 500 + 15), (1000, 128), jnp.float32)
        tbl_16 = 0.05 * jax.random.normal(jax.random.fold_in(_tk, 500 + 16), (12500, 128), jnp.float32)
        tbl_17 = 0.05 * jax.random.normal(jax.random.fold_in(_tk, 500 + 17), (12500, 128), jnp.float32)
        tbl_18 = 0.05 * jax.random.normal(jax.random.fold_in(_tk, 500 + 18), (12500, 128), jnp.float32)
        tbl_19 = 0.05 * jax.random.normal(jax.random.fold_in(_tk, 500 + 19), (12500, 128), jnp.float32)
        tbl_20 = 0.05 * jax.random.normal(jax.random.fold_in(_tk, 500 + 20), (1000, 128), jnp.float32)
        tbl_21 = 0.05 * jax.random.normal(jax.random.fold_in(_tk, 500 + 21), (1250, 128), jnp.float32)
        tbl_22 = 0.05 * jax.random.normal(jax.random.fold_in(_tk, 500 + 22), (12500, 128), jnp.float32)
        tbl_23 = 0.05 * jax.random.normal(jax.random.fold_in(_tk, 500 + 23), (1250, 128), jnp.float32)
        tbl_24 = 0.05 * jax.random.normal(jax.random.fold_in(_tk, 500 + 24), (1000, 128), jnp.float32)
        tbl_25 = 0.05 * jax.random.normal(jax.random.fold_in(_tk, 500 + 25), (1250, 128), jnp.float32)
        _rk = jax.random.fold_in(_tk, 7)
        r_dense_features = -0.000520686 + 1.00062 * jax.random.normal(jax.random.fold_in(_rk, 101), (512, 128), jnp.float32)
        W_top1 = 0.0405887 * jax.random.normal(jax.random.fold_in(_tk, 801), (607, 512), jnp.float32)
        W_top2 = 0.0441942 * jax.random.normal(jax.random.fold_in(_tk, 802), (512, 256), jnp.float32)
        W_top3 = 0.0625 * jax.random.normal(jax.random.fold_in(_tk, 803), (256, 1), jnp.float32)
        b_top1 = jnp.zeros((512,), jnp.float32)
        b_top2 = jnp.zeros((256,), jnp.float32)
        return (r_dense_features, ids, tbl_0, tbl_1, tbl_2, tbl_3, tbl_4, tbl_5, tbl_6, tbl_7, tbl_8, tbl_9, tbl_10, tbl_11, tbl_12, tbl_13, tbl_14, tbl_15, tbl_16, tbl_17, tbl_18, tbl_19, tbl_20, tbl_21, tbl_22, tbl_23, tbl_24, tbl_25, W_top1, b_top1, W_top2, b_top2, W_top3)
    r_dense_features, ids, tbl_0, tbl_1, tbl_2, tbl_3, tbl_4, tbl_5, tbl_6, tbl_7, tbl_8, tbl_9, tbl_10, tbl_11, tbl_12, tbl_13, tbl_14, tbl_15, tbl_16, tbl_17, tbl_18, tbl_19, tbl_20, tbl_21, tbl_22, tbl_23, tbl_24, tbl_25, W_top1, b_top1, W_top2, b_top2, W_top3 = _rec_inputs()

    def _L0_rec_setup():
        import jax, jax.numpy as jnp
        import numpy as np
        F = 26
        N = F + 1
        _TRIU_I, _TRIU_J = np.triu_indices(N, k=1)
        key = jax.random.key(seed)
        k1, k2 = jax.random.split(key)
        B, D = (2048, 128)
        dense_features = jax.random.normal(k1, (B, D), dtype=jnp.float32)
        sparse_features = jax.random.normal(k2, (B, F, D), dtype=jnp.float32)
        return {'dense_features': dense_features, 'sparse_features': sparse_features}
    _L0_rec_all = _L0_rec_setup()
    _L0_rec_in = {k: v for k, v in _L0_rec_all.items() if k in ()}
    del _L0_rec_all
    return {'r_dense_features': r_dense_features, 'ids': ids, 'tbl_0': tbl_0, 'tbl_1': tbl_1, 'tbl_2': tbl_2, 'tbl_3': tbl_3, 'tbl_4': tbl_4, 'tbl_5': tbl_5, 'tbl_6': tbl_6, 'tbl_7': tbl_7, 'tbl_8': tbl_8, 'tbl_9': tbl_9, 'tbl_10': tbl_10, 'tbl_11': tbl_11, 'tbl_12': tbl_12, 'tbl_13': tbl_13, 'tbl_14': tbl_14, 'tbl_15': tbl_15, 'tbl_16': tbl_16, 'tbl_17': tbl_17, 'tbl_18': tbl_18, 'tbl_19': tbl_19, 'tbl_20': tbl_20, 'tbl_21': tbl_21, 'tbl_22': tbl_22, 'tbl_23': tbl_23, 'tbl_24': tbl_24, 'tbl_25': tbl_25, 'W_top1': W_top1, 'b_top1': b_top1, 'W_top2': W_top2, 'b_top2': b_top2, 'W_top3': W_top3}

def reference(r_dense_features, ids, tbl_0, tbl_1, tbl_2, tbl_3, tbl_4, tbl_5, tbl_6, tbl_7, tbl_8, tbl_9, tbl_10, tbl_11, tbl_12, tbl_13, tbl_14, tbl_15, tbl_16, tbl_17, tbl_18, tbl_19, tbl_20, tbl_21, tbl_22, tbl_23, tbl_24, tbl_25, W_top1, b_top1, W_top2, b_top2, W_top3):
    import jax
    import jax.numpy as jnp

    def _L0_rec_ref(dense_features, sparse_features):
        import jax, jax.numpy as jnp
        import numpy as np
        F = 26
        N = F + 1
        _TRIU_I, _TRIU_J = np.triu_indices(N, k=1)
        combined = jnp.concatenate([dense_features[:, None, :], sparse_features], axis=1)
        interactions = jnp.einsum('bnd,bmd->bnm', combined, combined)
        interactions_flat = interactions[:, _TRIU_I, _TRIU_J]
        return jnp.concatenate([dense_features, interactions_flat], axis=1)
    e = jnp.stack([tbl_0[ids[:, 0]], tbl_1[ids[:, 1]], tbl_2[ids[:, 2]], tbl_3[ids[:, 3]], tbl_4[ids[:, 4]], tbl_5[ids[:, 5]], tbl_6[ids[:, 6]], tbl_7[ids[:, 7]], tbl_8[ids[:, 8]], tbl_9[ids[:, 9]], tbl_10[ids[:, 10]], tbl_11[ids[:, 11]], tbl_12[ids[:, 12]], tbl_13[ids[:, 13]], tbl_14[ids[:, 14]], tbl_15[ids[:, 15]], tbl_16[ids[:, 16]], tbl_17[ids[:, 17]], tbl_18[ids[:, 18]], tbl_19[ids[:, 19]], tbl_20[ids[:, 20]], tbl_21[ids[:, 21]], tbl_22[ids[:, 22]], tbl_23[ids[:, 23]], tbl_24[ids[:, 24]], tbl_25[ids[:, 25]]], axis=1)
    z = _L0_rec_ref(r_dense_features, e)
    z = z.reshape(z.shape[0], -1)
    h = jnp.concatenate([z, r_dense_features], axis=1)
    h = jnp.maximum(h @ W_top1 + b_top1, 0.0)
    h = jnp.maximum(h @ W_top2 + b_top2, 0.0)
    y = h @ W_top3
    return y

_drawn_inputs = setup_inputs


def setup_inputs(seed=0):
    import zlib

    import numpy as np

    out = dict(_drawn_inputs(seed))
    spreads = {'b_top1': (0.0, 0.1), 'b_top2': (0.0, 0.1)}
    factors = {}
    for name, (base, spread) in spreads.items():
        noise = np.random.default_rng([zlib.crc32(name.encode()), seed]).standard_normal(out[name].shape)
        drawn = base * np.exp(spread * noise) if base else spread * noise
        out[name] = jnp.asarray(drawn.astype(out[name].dtype))
    for name, factor in factors.items():
        out[name] = (out[name] * factor).astype(out[name].dtype)
    return out
```

```python
from contextlib import ExitStack

import concourse.bass as bass
from concourse import mybir

ALU = mybir.AluOpType
ACT = mybir.ActivationFunctionType
F32 = mybir.dt.float32
I32 = mybir.dt.int32

P = 128
BATCH = 512
D = 128
FIELDS = 26
N = FIELDS + 1
NP_ = 32
TILES = BATCH // P
QUADS = 4
GROUPS = P // QUADS
H1, H2 = 512, 256

PAIR_TILES = -(-(N - 1) // QUADS)

FEATS_PER_BANK = 4
TGROUPS = -(-N // FEATS_PER_BANK)
UNIT = 8
UNITS = GROUPS // UNIT


def feats_of(q):
    return range(q * FEATS_PER_BANK, min(N, (q + 1) * FEATS_PER_BANK))


def slots_of(quad):
    return len(range(1 + quad, N, QUADS))


def dlrm_tower(nc, x, ids, tables, w_pair, w_dense, b1, w2, b2, w3, y):
    with ExitStack() as ctx:
        def sb(name, shape, dt=F32):
            return ctx.enter_context(nc.sbuf_tensor(name, shape, dt))

        def sem(name):
            return ctx.enter_context(nc.semaphore(name))

        idx = sb("idx", [P, TILES, FIELDS], I32)
        x_sb = sb("x_sb", [P, TILES, D])
        emb = sb("emb", [P, TILES, FIELDS, D])
        vT = sb("vT", [P, TILES, GROUPS, QUADS, NP_])
        xT = sb("xT", [P, TILES, P])
        ident = sb("ident", [P, P])
        zT = sb("zT", [P, TILES, PAIR_TILES, P])
        wp_sb = sb("wp_sb", [P, PAIR_TILES, H1])
        wd2_sb = sb("wd2_sb", [P, 2, H1])
        wd_sb = sb("wd_sb", [P, H1])
        b1_sb = sb("b1_sb", [P, H1 // P])
        w2_sb = sb("w2_sb", [P, H1 // P, H2])
        b2_sb = sb("b2_sb", [P, H2 // P])
        w3_sb = sb("w3_sb", [P, H2 // P])
        h1T = sb("h1T", [P, TILES, H1 // P, P])
        h2T = sb("h2T", [P, TILES, H2 // P, P])
        y_sb = sb("y_sb", [1, BATCH])

        ps_t = [ctx.enter_context(nc.psum_tensor(f"ps_t{i}", [P, FEATS_PER_BANK, P], F32)) for i in range(2)]
        ps_g = [ctx.enter_context(nc.psum_tensor(f"ps_g{i}", [P, UNIT, P], F32)) for i in range(2)]
        ps_act = ctx.enter_context(nc.psum_tensor("ps_act", [P, 4, P], F32))
        ps_dve = ctx.enter_context(nc.psum_tensor("ps_dve", [P, 4, P], F32))

        ids_in = sem("ids_in")
        x_in = sem("x_in")
        w1_in = sem("w1_in")
        w23_in = sem("w23_in")
        ident_zero = sem("ident_zero")
        ident_ready = sem("ident_ready")
        pads_ready = sem("pads_ready")
        gathered = [[sem(f"gathered_{t}_{q}") for q in range(TGROUPS)] for t in range(TILES)]
        transposed = sem("transposed")
        vT_dve = sem("vT_dve")
        vT_act = sem("vT_act")
        gram_done = sem("gram_done")
        gram_dve = sem("gram_dve")
        gram_act = sem("gram_act")
        wd_ready = sem("wd_ready")
        l1_for_act = sem("l1_for_act")
        l1_for_dve = sem("l1_for_dve")
        h1_dve = sem("h1_dve")
        h1_act = sem("h1_act")
        l2_for_act = sem("l2_for_act")
        l2_for_dve = sem("l2_for_dve")
        h2_dve = sem("h2_dve")
        h2_act = sem("h2_act")
        l3_done = sem("l3_done")
        y_ready = sem("y_ready")
        y_stored = sem("y_stored")

        def copied_by_dve(i):
            return i // 2 + 1

        def copied_by_act(i):
            return (i + 1) // 2

        block = ctx.enter_context(nc.Block())

        @block.sync
        def _(sp):
            sp.dma_start(idx[:], ids.rearrange("(t p) f -> p t f", p=P)).then_inc(ids_in, 16)
            sp.dma_start(x_sb[:], x.rearrange("(t p) d -> p t d", p=P)).then_inc(x_in, 16)
            sp.dma_start(wp_sb[:], w_pair).then_inc(w1_in, 16)
            sp.dma_start(wd2_sb[:], w_dense.rearrange("a r o -> r a o")).then_inc(w1_in, 16)
            sp.dma_start(b1_sb[:], b1).then_inc(w1_in, 16)
            sp.dma_start(w2_sb[:], w2.rearrange("(c r) o -> r c o", r=P)).then_inc(w23_in, 16)
            sp.dma_start(b2_sb[:], b2).then_inc(w23_in, 16)
            sp.dma_start(w3_sb[:], w3).then_inc(w23_in, 16)
            sp.wait_ge(y_ready, TILES)
            sp.dma_start(y, y_sb[:]).then_inc(y_stored, 16)
            sp.wait_ge(y_stored, 16)

        @block.gpsimd
        def _(pool):
            nc.gpsimd.memset(ident[:], 0.0).then_inc(ident_zero, 1)
            pool.wait_ge(ident_zero, 1)
            nc.gpsimd.affine_select(out=ident[:], in_=ident[:], compare_op=ALU.not_equal, fill=1.0, base=0,
                                    pattern=[[-1, P]], channel_multiplier=1).then_inc(ident_ready, 1)
            for t in range(TILES):
                if t == 0:
                    pool.wait_ge(ids_in, 16)
                for q in range(TGROUPS):
                    for n in feats_of(q):
                        if n == 0:
                            continue
                        f = n - 1
                        nc.gpsimd.indirect_dma_start(
                            out=emb[:, t, f, :], out_offset=None, in_=tables[f],
                            in_offset=bass.IndirectOffsetOnAxis(ap=idx[:, t, f:f + 1], axis=0)
                        ).then_inc(gathered[t][q], 16)

        @block.tensor
        def _(pe):
            def transpose_bank(t, q):
                i = TGROUPS * t + q
                if i >= 2:
                    if i % 2 == 0:
                        pe.wait_ge(vT_dve, copied_by_dve(i - 2))
                    else:
                        pe.wait_ge(vT_act, copied_by_act(i - 2))
                if q == 0:
                    pe.wait_ge(x_in, 16)
                pe.wait_ge(gathered[t][q], 16 * len([n for n in feats_of(q) if n > 0]))
                for s, n in enumerate(feats_of(q)):
                    src = x_sb[:, t, :] if n == 0 else emb[:, t, n - 1, :]
                    last = nc.tensor.transpose(ps_t[i % 2][:, s, :], src, ident[:])
                last.then_inc(transposed, 1)

            def grams(t):
                i = TGROUPS * (t + 1) - 1
                pe.wait_ge(vT_dve, copied_by_dve(i))
                pe.wait_ge(vT_act, copied_by_act(i))
                for u in range(UNITS):
                    k = UNITS * t + u
                    if k >= 2:
                        pe.wait_ge(gram_dve, k - 1)
                        pe.wait_ge(gram_act, k - 1)
                    for g in range(UNIT):
                        v = vT[:, t, u * UNIT + g, :, :]
                        out = ps_g[k % 2][:, g, 0:QUADS * N].rearrange("p (j m) -> p j m", j=QUADS)
                        last = nc.tensor.matmul(out, v.rearrange("p j n -> p (j n)"), v[:, :, 0:N],
                                                start=True, stop=True)
                    last.then_inc(gram_done, 1)

            def tower(t):
                if t == 0:
                    pe.wait_ge(w1_in, 48)
                    pe.wait_ge(wd_ready, 1)
                pe.wait_ge(gram_dve, UNITS * (t + 1))
                pe.wait_ge(gram_act, UNITS * (t + 1))
                for c in range(H1 // P):
                    if t >= 1 and c == 0:
                        pe.wait_ge(y_ready, t)
                    if t >= 1 and c == 2:
                        pe.wait_ge(h2_dve, t)
                    cols = slice(c * P, (c + 1) * P)
                    out = (ps_act, ps_dve)[c // 2][:, c % 2, :]
                    nc.tensor.matmul(out, wd_sb[:, cols], xT[:, t, :], start=True, stop=False)
                    for i in range(PAIR_TILES):
                        last = nc.tensor.matmul(out, wp_sb[:, i, cols], zT[:, t, i, :],
                                                start=False, stop=(i == PAIR_TILES - 1))
                    if c % 2 == 1:
                        last.then_inc((l1_for_act, l1_for_dve)[c // 2], 1)
                if t == 0:
                    pe.wait_ge(w23_in, 48)
                pe.wait_ge(h1_act, t + 1)
                pe.wait_ge(h1_dve, t + 1)
                for c in range(H2 // P):
                    for k in range(H1 // P):
                        last = nc.tensor.matmul((ps_act, ps_dve)[c][:, 2, :], w2_sb[:, k, c * P:(c + 1) * P],
                                                h1T[:, t, k, :], start=(k == 0), stop=(k == H1 // P - 1))
                    last.then_inc((l2_for_act, l2_for_dve)[c], 1)
                pe.wait_ge(h2_act, t + 1)
                pe.wait_ge(h2_dve, t + 1)
                for k in range(H2 // P):
                    last = nc.tensor.matmul(ps_act[0:1, 3, :], w3_sb[:, k:k + 1], h2T[:, t, k, :],
                                            start=(k == 0), stop=(k == H2 // P - 1))
                last.then_inc(l3_done, 1)

            pe.wait_ge(ident_ready, 1)
            for t in range(TILES):
                for q in range(TGROUPS):
                    transpose_bank(t, q)
                    if t >= 1 and q == 3:
                        tower(t - 1)
                if t == 0:
                    pe.wait_ge(pads_ready, 2)
                grams(t)
            tower(TILES - 1)

        def copy_transposes(eng, copy, ready, t, q):
            i = TGROUPS * t + q
            eng.wait_ge(transposed, i + 1)
            fs = feats_of(q)
            src = ps_t[i % 2][:, 0:len(fs), :].rearrange("p f (j g) -> p f j g", j=QUADS)
            dst = vT[:, t, :, :, fs[0]:fs[-1] + 1].rearrange("p g j f -> p f j g")
            if q == 0:
                copy(xT[:, t, :], ps_t[i % 2][:, 0, :])
            copy(dst, src).then_inc(ready, 1)

        def copy_grams(eng, copy, ready, quads, t, u):
            k = UNITS * t + u
            eng.wait_ge(gram_done, k + 1)
            for j in quads:
                for jj in range(QUADS):
                    m0 = j * N + 1 + jj
                    m1 = m0 + QUADS * (slots_of(jj) - 1) + 1
                    src = ps_g[k % 2][NP_ * j:NP_ * (j + 1), :, m0:m1:QUADS].rearrange("p g s -> p s g")
                    b0 = GROUPS * j + u * UNIT
                    last = copy(zT[NP_ * jj:NP_ * (jj + 1), t, 0:slots_of(jj), b0:b0 + UNIT], src)
            last.then_inc(ready, 1)

        @block.scalar
        def _(act):
            def copy(dst, src):
                return nc.scalar.activation(dst, src, ACT.Copy)

            def tower(t):
                act.wait_ge(l1_for_act, t + 1)
                for c in (0, 1):
                    last = nc.scalar.activation(h1T[:, t, c, :], ps_act[:, c, :], ACT.Relu, bias=b1_sb[:, c:c + 1])
                last.then_inc(h1_act, 1)
                act.wait_ge(l2_for_act, t + 1)
                nc.scalar.activation(h2T[:, t, 0, :], ps_act[:, 2, :], ACT.Relu, bias=b2_sb[:, 0:1])\
                    .then_inc(h2_act, 1)
                act.wait_ge(l3_done, t + 1)
                nc.scalar.activation(y_sb[0:1, t * P:(t + 1) * P], ps_act[0:1, 3, :], ACT.Copy).then_inc(y_ready, 1)

            act.wait_ge(w1_in, 48)
            act.wait_ge(w23_in, 48)
            for t in range(TILES):
                for q in range(TGROUPS):
                    if (TGROUPS * t + q) % 2 == 1:
                        copy_transposes(act, copy, vT_act, t, q)
                    if t >= 1 and q == 3:
                        tower(t - 1)
                for u in range(UNITS):
                    copy_grams(act, copy, gram_act, (2, 3), t, u)
            tower(TILES - 1)

        @block.vector
        def _(dve):
            def copy(dst, src):
                return nc.vector.tensor_copy(dst, src)

            def tower(t):
                dve.wait_ge(l1_for_dve, t + 1)
                for c in (2, 3):
                    last = nc.vector.tensor_scalar(h1T[:, t, c, :], ps_dve[:, c - 2, :], b1_sb[:, c:c + 1], 0.0,
                                                   ALU.add, ALU.max)
                last.then_inc(h1_dve, 1)
                dve.wait_ge(l2_for_dve, t + 1)
                nc.vector.tensor_scalar(h2T[:, t, 1, :], ps_dve[:, 2, :], b2_sb[:, 1:2], 0.0, ALU.add, ALU.max)\
                    .then_inc(h2_dve, 1)

            nc.vector.memset(vT[:, :, :, :, N:NP_], 0.0).then_inc(pads_ready, 1)
            nc.vector.memset(zT[2 * NP_:P, :, PAIR_TILES - 1, :], 0.0).then_inc(pads_ready, 1)
            dve.wait_ge(w1_in, 48)
            nc.vector.tensor_tensor(wd_sb[:], wd2_sb[:, 0, :], wd2_sb[:, 1, :], ALU.add).then_inc(wd_ready, 1)
            dve.wait_ge(w23_in, 48)
            for t in range(TILES):
                for q in range(TGROUPS):
                    if (TGROUPS * t + q) % 2 == 0:
                        copy_transposes(dve, copy, vT_dve, t, q)
                    if t >= 1 and q == 3:
                        tower(t - 1)
                for u in range(UNITS):
                    copy_grams(dve, copy, gram_dve, (0, 1), t, u)
            tower(TILES - 1)


def kernel(**inputs):
    import numpy as np
    import concourse.bacc as bacc
    from concourse.bass_utils import run_bass_kernel_spmd

    w_top1 = np.asarray(inputs["W_top1"])
    pairs = N * (N - 1) // 2
    w_pair = np.zeros((QUADS, NP_, PAIR_TILES, H1), w_top1.dtype)
    for m in range(1, N):
        s, jj = divmod(m - 1, QUADS)
        w_pair[jj, :m, s] = w_top1[[D + n * (2 * N - n - 1) // 2 + (m - n - 1) for n in range(m)]]
    arrays = {
        "x": np.asarray(inputs["r_dense_features"]),
        "ids": np.asarray(inputs["ids"]),
        "w_pair": w_pair.reshape(P, PAIR_TILES, H1),
        "w_dense": np.stack([w_top1[0:D], w_top1[D + pairs:]]),
        "b1": np.asarray(inputs["b_top1"]).reshape(H1 // P, P).T,
        "w2": np.asarray(inputs["W_top2"]),
        "b2": np.asarray(inputs["b_top2"]).reshape(H2 // P, P).T,
        "w3": np.asarray(inputs["W_top3"]).reshape(H2 // P, P).T,
    }
    for f in range(FIELDS):
        arrays[f"tbl_{f}"] = np.asarray(inputs[f"tbl_{f}"])
    arrays = {f"in_{k}": np.ascontiguousarray(a) for k, a in arrays.items()}

    nc = bacc.Bacc("TRN2", target_bir_lowering=False, num_devices=1)
    ap = {k: nc.dram_tensor(k, a.shape, mybir.dt.from_np(a.dtype), kind="ExternalInput").ap()
          for k, a in arrays.items()}
    y = nc.dram_tensor("out_y", (BATCH, 1), F32, kind="ExternalOutput").ap()
    dlrm_tower(nc, ap["in_x"], ap["in_ids"], [ap[f"in_tbl_{f}"] for f in range(FIELDS)], ap["in_w_pair"],
               ap["in_w_dense"], ap["in_b1"], ap["in_w2"], ap["in_b2"], ap["in_w3"],
               y.rearrange("b a -> a b"))
    r = run_bass_kernel_spmd(nc, [arrays], core_ids=[0])
    return r.results[0]["out_y"]
```

```python
from contextlib import ExitStack

import concourse.bass as bass
from concourse import mybir

ALU = mybir.AluOpType
ACT = mybir.ActivationFunctionType
F32 = mybir.dt.float32
F16 = mybir.dt.float16
F32R = mybir.dt.float32r
I32 = mybir.dt.int32

P = 128
BATCH = 512
D = 128
FIELDS = 26
N = FIELDS + 1
NP_ = 32
TILES = BATCH // P
QUADS = 4
GROUPS = P // QUADS
H1, H2 = 512, 256

TABLE_ROWS = [1000, 1000, 1000, 1250, 1250, 125000, 1000, 1000, 1000, 12500, 1000, 1250, 1250,
              12500, 12500, 1000, 12500, 12500, 12500, 12500, 1000, 1250, 12500, 1250, 1000, 1250]
CHUNKS = 8
PICKED_ROWS = 1000
PICKED = [f for f in range(FIELDS) if TABLE_ROWS[f] == PICKED_ROWS][:6]
GATHERED = [f for f in range(FIELDS) if f not in PICKED]
ROWS_PER_CHUNK = PICKED_ROWS // CHUNKS
K = len(PICKED)
FIELD_AT = [None] + PICKED + GATHERED

PAIR_TILES = -(-(N - 1) // QUADS)

FEATS_PER_BANK = 4
BANKS_OF = [[0]] + [list(range(a, min(N, a + FEATS_PER_BANK))) for a in range(K + 1, N, FEATS_PER_BANK)]
TGROUPS = len(BANKS_OF)
UNIT = 8
UNITS = GROUPS // UNIT
CHUNKS_BY_ACT = 2


def schedule():
    steps = [("bank", 0, 0), ("pick", 0, 0)]
    for i in range(1, max(TGROUPS, K)):
        steps += [("pick", 0, i)] * (i < K) + [("bank", 0, i)] * (i < TGROUPS)
    for t in range(TILES):
        behind_unit = {0: [("layer2", t - 1, 0)], 1: [("layer3", t - 1, 0)]} if 1 <= t < TILES - 1 else {}
        for u in range(UNITS):
            steps += [("grams", t, u)] + behind_unit.get(u, [])
        banks = [("bank", t + 1, q) for q in range(TGROUPS)] if t < TILES - 1 else []
        late = banks[-2:] if t == TILES - 2 else []
        early = banks[:len(banks) - len(late)]
        steps += early[0:1] + [("dense", t, 0)] + early[1:2] + [("layer1", t, 0)] + early[2:3]
        steps += [("layer1", t, 1)] + early[3:4] + [("layer1", t, 2)] + early[4:] + [("layer1", t, 3)]
        if t >= TILES - 2:
            steps += [("layer2", t, 0)] + late[0:1] + [("layer3", t, 0)] + late[1:2]
    return steps


SCHEDULE = schedule()
assert len(set(SCHEDULE)) == len(SCHEDULE)


def copies_by_act(t, q):
    return t == 0 or (TGROUPS * t + q) % 2 == 1


def copies_until(t, q, by_act):
    return sum(copies_by_act(*divmod(i, TGROUPS)) == by_act for i in range(TGROUPS * t + q + 1))


def slots_of(quad):
    return len(range(1 + quad, N, QUADS))


def dlrm_tower(nc, x, ids, ids_by_field, tables, w_pair, w_dense, b1, w2, b2, w3, y):
    with ExitStack() as ctx:
        def sb(name, shape, dt=F32):
            return ctx.enter_context(nc.sbuf_tensor(name, shape, dt))

        def sem(name):
            return ctx.enter_context(nc.semaphore(name))

        idx = sb("idx", [P, TILES, FIELDS], I32)
        row0_i = sb("row0_i", [ROWS_PER_CHUNK, 1], I32)
        row0 = sb("row0", [ROWS_PER_CHUNK, 1])
        ids_bc = sb("ids_bc", [ROWS_PER_CHUNK, 2, BATCH], I32)
        minus_row = sb("minus_row", [ROWS_PER_CHUNK, CHUNKS])
        distance = sb("distance", [ROWS_PER_CHUNK, BATCH])
        ids_h = sb("ids_h", [ROWS_PER_CHUNK, 2, BATCH], F16)
        table = sb("table", [ROWS_PER_CHUNK, 2, CHUNKS, D])
        table_hi = sb("table_hi", [ROWS_PER_CHUNK, 2, CHUNKS, D], F32R)
        table_lo = sb("table_lo", [ROWS_PER_CHUNK, 2, CHUNKS, D], F32R)
        onehot = sb("onehot", [ROWS_PER_CHUNK, 2, CHUNKS, BATCH], F32R)
        x_sb = sb("x_sb", [P, TILES, D])
        emb = sb("emb", [P, 2, len(GATHERED), D])
        vT = sb("vT", [P, TILES, GROUPS, QUADS, NP_])
        xT = sb("xT", [P, TILES, P])
        ident = sb("ident", [P, P])
        zT = sb("zT", [P, TILES, PAIR_TILES, P])
        wp_sb = sb("wp_sb", [P, PAIR_TILES, H1])
        wd2_sb = sb("wd2_sb", [P, 2, H1])
        wd_sb = sb("wd_sb", [P, H1])
        b1_sb = sb("b1_sb", [P, H1 // P])
        w2_sb = sb("w2_sb", [P, H1 // P, H2])
        b2_sb = sb("b2_sb", [P, H2 // P])
        w3_sb = sb("w3_sb", [P, H2 // P])
        h1T = sb("h1T", [P, H1 // P, P])
        h2T = sb("h2T", [P, H2 // P, P])
        y_sb = sb("y_sb", [1, BATCH])

        ps_t = [ctx.enter_context(nc.psum_tensor(f"ps_t{i}", [P, FEATS_PER_BANK, P], F32)) for i in range(2)]
        ps_g = [ctx.enter_context(nc.psum_tensor(f"ps_g{i}", [P, UNIT, P], F32)) for i in range(2)]
        ps_act = ctx.enter_context(nc.psum_tensor("ps_act", [P, 4, P], F32))
        ps_dve = ctx.enter_context(nc.psum_tensor("ps_dve", [P, 4, P], F32))

        ids_in = sem("ids_in")
        x_in = sem("x_in")
        w1_in = sem("w1_in")
        w23_in = sem("w23_in")
        ident_zero = sem("ident_zero")
        ident_ready = sem("ident_ready")
        pads_ready = sem("pads_ready")
        gathered = [[sem(f"gathered_{t}_{q}") for q in range(TGROUPS)] for t in range(TILES)]
        ids_bc_in = [sem(f"ids_bc_in{o}") for o in range(K)]
        table_in = [sem(f"table_in{o}") for o in range(K)]
        row0_int = sem("row0_int")
        row0_ready = sem("row0_ready")
        ids_h_ready = sem("ids_h_ready")
        minus_row_ready = sem("minus_row_ready")
        onehot_dve = sem("onehot_dve")
        distance_ready = sem("distance_ready")
        onehot_act = sem("onehot_act")
        hi_ready = sem("hi_ready")
        lo_ready = sem("lo_ready")
        picked = sem("picked")
        picked_act = sem("picked_act")
        transposed = sem("transposed")
        vT_dve = sem("vT_dve")
        vT_act = sem("vT_act")
        gram_done = sem("gram_done")
        gram_dve = sem("gram_dve")
        gram_act = sem("gram_act")
        wd_ready = sem("wd_ready")
        l1_for_act = sem("l1_for_act")
        l1_for_dve = sem("l1_for_dve")
        h1_dve = sem("h1_dve")
        h1_act = sem("h1_act")
        l2_for_act = sem("l2_for_act")
        l2_for_dve = sem("l2_for_dve")
        h2_dve = sem("h2_dve")
        h2_act = sem("h2_act")
        l3_done = sem("l3_done")
        y_ready = sem("y_ready")
        y_stored = sem("y_stored")

        ps_o = [ps_g[i][:, 0:UNIT // 2, :] for i in range(2)]

        def table_rows(o):
            return tables[PICKED[o]].rearrange("(p c) d -> p c d", c=CHUNKS)

        block = ctx.enter_context(nc.Block())

        @block.sync
        def _(sp):
            sp.dma_start(idx[:], ids.rearrange("(t p) f -> p t f", p=P)).then_inc(ids_in, 16)

            def load_table(o):
                if o >= 2:
                    sp.wait_ge(ids_h_ready, o - 1)
                sp.dma_start(ids_bc[:, o % 2, :], ids_by_field[PICKED[o]:PICKED[o] + 1, :]
                             .broadcast_to([ROWS_PER_CHUNK, BATCH])).then_inc(ids_bc_in[o], 16)
                if o >= 2:
                    sp.wait_ge(lo_ready, o - 1)
                if o > 0:
                    sp.dma_start(table[:, o % 2, :, :], table_rows(o)).then_inc(table_in[o], 16)

            load_table(0)
            sp.dma_start(x_sb[:], x.rearrange("(t p) d -> p t d", p=P)).then_inc(x_in, 16)
            load_table(1)
            sp.dma_start(wp_sb[:], w_pair).then_inc(w1_in, 16)
            sp.dma_start(wd2_sb[:], w_dense.rearrange("a r o -> r a o")).then_inc(w1_in, 16)
            sp.dma_start(b1_sb[:], b1).then_inc(w1_in, 16)
            sp.dma_start(w2_sb[:], w2.rearrange("(c r) o -> r c o", r=P)).then_inc(w23_in, 16)
            sp.dma_start(b2_sb[:], b2).then_inc(w23_in, 16)
            sp.dma_start(w3_sb[:], w3).then_inc(w23_in, 16)
            for o in range(2, K):
                load_table(o)
            sp.wait_ge(y_ready, TILES)
            sp.dma_start(y, y_sb[:]).then_inc(y_stored, 16)
            sp.wait_ge(y_stored, 16)

        @block.gpsimd
        def _(pool):
            nc.gpsimd.memset(ident[:], 0.0).then_inc(ident_zero, 1)
            pool.wait_ge(ident_zero, 1)
            nc.gpsimd.affine_select(out=ident[:], in_=ident[:], compare_op=ALU.not_equal, fill=1.0, base=0,
                                    pattern=[[-1, P]], channel_multiplier=1).then_inc(ident_ready, 1)
            nc.gpsimd.iota(row0_i[:], pattern=[[0, 1]], base=0, channel_multiplier=CHUNKS).then_inc(row0_int, 1)
            for t in range(TILES):
                if t == 0:
                    pool.wait_ge(ids_in, 16)
                for q in range(1, TGROUPS):
                    if t >= 2:
                        pool.wait_ge(transposed, TGROUPS * (t - 2) + q + 1)
                    for n in BANKS_OF[q]:
                        f = FIELD_AT[n]
                        nc.gpsimd.indirect_dma_start(
                            out=emb[:, t % 2, n - K - 1, :], out_offset=None, in_=tables[f],
                            in_offset=bass.IndirectOffsetOnAxis(ap=idx[:, t, f:f + 1], axis=0)
                        ).then_inc(gathered[t][q], 16)

        @block.tensor
        def _(pe):
            def pick(o):
                if o >= 2:
                    pe.wait_ge(picked_act, o - 1)
                pe.wait_ge(hi_ready, o + 1)
                pe.wait_ge(lo_ready, o + 1)
                for c in range(CHUNKS):
                    by_act = c - (CHUNKS - CHUNKS_BY_ACT)
                    if by_act < 0:
                        pe.wait_ge(onehot_dve, (CHUNKS - CHUNKS_BY_ACT) * o + c + 1)
                    else:
                        pe.wait_ge(onehot_act, CHUNKS_BY_ACT * o + by_act + 1)
                    nc.tensor.matmul(ps_o[o % 2], table_hi[:, o % 2, c, :], onehot[:, o % 2, c, :],
                                     start=(c == 0), stop=False)
                    nc.tensor.matmul(ps_o[o % 2], table_lo[:, o % 2, c, :], onehot[:, o % 2, c, :],
                                     start=False, stop=(c == CHUNKS - 1)).then_inc(picked, 1)

            def transpose_bank(t, q):
                i = TGROUPS * t + q
                if i >= 2:
                    t2, q2 = divmod(i - 2, TGROUPS)
                    by_act = copies_by_act(t2, q2)
                    pe.wait_ge(vT_act if by_act else vT_dve, copies_until(t2, q2, by_act))
                if i == 0:
                    pe.wait_ge(x_in, 16)
                if q > 0:
                    pe.wait_ge(gathered[t][q], 16 * len(BANKS_OF[q]))
                for s, n in enumerate(BANKS_OF[q]):
                    src = x_sb[:, t, :] if n == 0 else emb[:, t % 2, n - K - 1, :]
                    last = nc.tensor.transpose(ps_t[i % 2][:, s, :], src, ident[:])
                last.then_inc(transposed, 1)

            def grams(t, u):
                if t == 0 and u == 0:
                    pe.wait_ge(pads_ready, 2)
                    pe.wait_ge(picked_act, K)
                if u == 0:
                    for by_act in (False, True):
                        n = copies_until(t, TGROUPS - 1, by_act)
                        if n:
                            pe.wait_ge(vT_act if by_act else vT_dve, n)
                k = UNITS * t + u
                if k >= 2:
                    pe.wait_ge(gram_dve, k - 1)
                    pe.wait_ge(gram_act, k - 1)
                for g in range(UNIT):
                    v = vT[:, t, u * UNIT + g, :, :]
                    out = ps_g[k % 2][:, g, 0:QUADS * (N - 1)].rearrange("p (j m) -> p j m", j=QUADS)
                    last = nc.tensor.matmul(out, v.rearrange("p j n -> p (j n)"), v[:, :, 1:N],
                                            start=True, stop=True)
                last.then_inc(gram_done, 1)

            def first_layer_sum(c):
                return (ps_act, ps_dve)[c // 2][:, c % 2, :]

            def dense(t):
                if t == 0:
                    pe.wait_ge(w1_in, 48)
                    pe.wait_ge(wd_ready, 1)
                for c in range(H1 // P):
                    if c == 0 and t >= 1:
                        pe.wait_ge(y_ready, t)
                    if c == 2 and t >= 1:
                        pe.wait_ge(h2_dve, t)
                    nc.tensor.matmul(first_layer_sum(c), wd_sb[:, c * P:(c + 1) * P], xT[:, t, :],
                                     start=(c % 2 == 0), stop=False, skip_group_check=True)

            def layer1(t, c):
                if c == 0:
                    pe.wait_ge(gram_dve, UNITS * (t + 1))
                    pe.wait_ge(gram_act, UNITS * (t + 1))
                for s in range(PAIR_TILES):
                    last = nc.tensor.matmul(first_layer_sum(c), wp_sb[:, s, c * P:(c + 1) * P], zT[:, t, s, :],
                                            start=False, stop=(s == PAIR_TILES - 1), skip_group_check=True)
                if c % 2 == 1:
                    last.then_inc((l1_for_act, l1_for_dve)[c // 2], 1)

            def layer2(t):
                if t == 0:
                    pe.wait_ge(w23_in, 48)
                pe.wait_ge(h1_act, t + 1)
                for c in range(H2 // P):
                    for k in range(H1 // P):
                        if c == 0 and k == 2:
                            pe.wait_ge(h1_dve, t + 1)
                        last = nc.tensor.matmul((ps_act, ps_dve)[c][:, 2, :], w2_sb[:, k, c * P:(c + 1) * P],
                                                h1T[:, k, :], start=(k == 0), stop=(k == H1 // P - 1))
                    last.then_inc((l2_for_act, l2_for_dve)[c], 1)

            def layer3(t):
                pe.wait_ge(h2_act, t + 1)
                for k in range(H2 // P):
                    if k == 1:
                        pe.wait_ge(h2_dve, t + 1)
                    last = nc.tensor.matmul(ps_act[0:1, 3, :], w3_sb[:, k:k + 1], h2T[:, k, :],
                                            start=(k == 0), stop=(k == H2 // P - 1))
                last.then_inc(l3_done, 1)

            pe.wait_ge(ident_ready, 1)
            for kind, t, i in SCHEDULE:
                if kind == "pick":
                    pick(i)
                elif kind == "bank":
                    transpose_bank(t, i)
                elif kind == "grams":
                    grams(t, i)
                elif kind == "dense":
                    dense(t)
                elif kind == "layer1":
                    layer1(t, i)
                elif kind == "layer2":
                    layer2(t)
                elif kind == "layer3":
                    layer3(t)

        def copy_transposes(eng, copy, ready, t, q):
            i = TGROUPS * t + q
            eng.wait_ge(transposed, i + 1)
            fs = BANKS_OF[q]
            src = ps_t[i % 2][:, 0:len(fs), :].rearrange("p f (j g) -> p f j g", j=QUADS)
            dst = vT[:, t, :, :, fs[0]:fs[-1] + 1].rearrange("p g j f -> p f j g")
            if q == 0:
                copy(xT[:, t, :], ps_t[i % 2][:, 0, :])
            copy(dst, src).then_inc(ready, 1)

        def copy_grams(eng, copy, ready, quads, t, u):
            k = UNITS * t + u
            eng.wait_ge(gram_done, k + 1)
            for j in quads:
                for jj in range(QUADS):
                    ns = slots_of(jj)
                    c0 = j * (N - 1) + jj
                    src = ps_g[k % 2][NP_ * j:NP_ * (j + 1), :, c0:c0 + QUADS * (ns - 1) + 1:QUADS]
                    b0 = GROUPS * j + u * UNIT
                    last = copy(zT[NP_ * jj:NP_ * (jj + 1), t, 0:ns, b0:b0 + UNIT],
                                src.rearrange("p g s -> p s g"))
            last.then_inc(ready, 1)

        @block.scalar
        def _(act):
            def copy(dst, src):
                return nc.scalar.activation(dst, src, ACT.Copy)

            def follow(kind, t, i):
                if kind == "pick":
                    if i == 0:
                        split_hi(0)
                        make_onehot(0)
                    if i + 1 < K:
                        split_hi(i + 1)
                        make_onehot(i + 1)
                    act.wait_ge(picked, CHUNKS * (i + 1))
                    src = ps_o[i % 2].rearrange("p t (j g) -> p t j g", j=QUADS)
                    copy(vT[:, :, :, :, 1 + i].rearrange("p t g j -> p t j g"), src).then_inc(picked_act, 1)
                if kind == "bank" and copies_by_act(t, i):
                    copy_transposes(act, copy, vT_act, t, i)
                if kind == "grams":
                    copy_grams(act, copy, gram_act, (2, 3), t, i)
                if (kind, t, i) == ("layer1", 0, 0):
                    act.wait_ge(w1_in, 48)
                    act.wait_ge(w23_in, 48)
                if kind == "layer1" and i == 1:
                    act.wait_ge(l1_for_act, t + 1)
                    if t >= 1:
                        act.wait_ge(l2_for_dve, t)
                    for c in (0, 1):
                        last = nc.scalar.activation(h1T[:, c, :], ps_act[:, c, :], ACT.Relu, bias=b1_sb[:, c:c + 1])
                    last.then_inc(h1_act, 1)
                if kind == "layer2":
                    act.wait_ge(l2_for_act, t + 1)
                    nc.scalar.activation(h2T[:, 0, :], ps_act[:, 2, :], ACT.Relu, bias=b2_sb[:, 0:1])\
                        .then_inc(h2_act, 1)
                if kind == "layer3":
                    act.wait_ge(l3_done, t + 1)
                    nc.scalar.activation(y_sb[0:1, t * P:(t + 1) * P], ps_act[0:1, 3, :], ACT.Copy)\
                        .then_inc(y_ready, 1)

            act.dma_start(table[:, 0, :, :], table_rows(0)).then_inc(table_in[0], 16)

            def make_onehot(o):
                act.wait_ge(ids_h_ready, o + 1)
                if o == 0:
                    act.wait_ge(minus_row_ready, 1)
                for i in range(CHUNKS_BY_ACT):
                    c = CHUNKS - CHUNKS_BY_ACT + i
                    done = CHUNKS_BY_ACT * o + i
                    if o >= 2:
                        act.wait_ge(picked, CHUNKS * (o - 2) + c + 1)
                    if done > 0:
                        act.wait_ge(onehot_act, done)
                    nc.scalar.activation(distance[:], ids_h[:, o % 2, :], ACT.Abs, bias=minus_row[:, c:c + 1])\
                        .then_inc(distance_ready, 1)
                    act.wait_ge(distance_ready, done + 1)
                    nc.scalar.activation(onehot[:, o % 2, c, :], distance[:], ACT.Relu, bias=1.0, scale=-1.0)\
                        .then_inc(onehot_act, 1)

            def split_hi(o):
                act.wait_ge(table_in[o], 16)
                if o >= 2:
                    act.wait_ge(picked, CHUNKS * (o - 1))
                copy(table_hi[:, o % 2], table[:, o % 2]).then_inc(hi_ready, 1)

            for kind, t, i in SCHEDULE:
                follow(kind, t, i)

        @block.vector
        def _(dve):
            def copy(dst, src):
                return nc.vector.tensor_copy(dst, src)

            def follow(kind, t, i):
                if kind == "bank" and not copies_by_act(t, i):
                    copy_transposes(dve, copy, vT_dve, t, i)
                if kind == "grams":
                    copy_grams(dve, copy, gram_dve, (0, 1), t, i)
                if kind == "layer1" and i == 3:
                    dve.wait_ge(l1_for_dve, t + 1)
                    for c in (2, 3):
                        last = nc.vector.tensor_scalar(h1T[:, c, :], ps_dve[:, c - 2, :], b1_sb[:, c:c + 1], 0.0,
                                                       ALU.add, ALU.max)
                    last.then_inc(h1_dve, 1)
                if kind == "layer2":
                    dve.wait_ge(l2_for_dve, t + 1)
                    if t >= 1:
                        dve.wait_ge(l3_done, t)
                    nc.vector.tensor_scalar(h2T[:, 1, :], ps_dve[:, 2, :], b2_sb[:, 1:2], 0.0, ALU.add, ALU.max)\
                        .then_inc(h2_dve, 1)

            nc.vector.memset(vT[:, :, :, :, N:NP_], 0.0).then_inc(pads_ready, 1)
            dve.wait_ge(row0_int, 1)
            nc.vector.tensor_copy(row0[:], row0_i[:]).then_inc(row0_ready, 1)
            dve.wait_ge(row0_ready, 1)
            for c in range(CHUNKS):
                last = nc.vector.tensor_scalar(minus_row[:, c:c + 1], row0[:], -1.0, -float(c), ALU.mult, ALU.add)
            last.then_inc(minus_row_ready, 1)
            for o in range(K):
                dve.wait_ge(ids_bc_in[o], 16)
                if o >= 2:
                    dve.wait_ge(onehot_act, CHUNKS_BY_ACT * (o - 1))
                nc.vector.tensor_copy(ids_h[:, o % 2, :], ids_bc[:, o % 2, :]).then_inc(ids_h_ready, 1)
                dve.wait_ge(table_in[o], 16)
                dve.wait_ge(hi_ready, o + 1)
                if o >= 2:
                    dve.wait_ge(picked, CHUNKS * (o - 1))
                nc.vector.tensor_tensor(table_lo[:, o % 2], table[:, o % 2], table_hi[:, o % 2].bitcast(F32),
                                        ALU.subtract).then_inc(lo_ready, 1)
                dve.wait_ge(ids_h_ready, o + 1)
                for c in range(CHUNKS - CHUNKS_BY_ACT):
                    if o >= 2:
                        dve.wait_ge(picked, CHUNKS * (o - 2) + c + 1)
                    nc.vector.tensor_scalar(onehot[:, o % 2, c, :], ids_h[:, o % 2, :], float(c), row0[:, 0:1],
                                            ALU.subtract, ALU.is_equal).then_inc(onehot_dve, 1)
                if o == 1:
                    dve.wait_ge(w1_in, 48)
                    nc.vector.tensor_tensor(wd_sb[:], wd2_sb[:, 0, :], wd2_sb[:, 1, :], ALU.add).then_inc(wd_ready, 1)
            nc.vector.memset(zT[2 * NP_:P, :, PAIR_TILES - 1, :], 0.0).then_inc(pads_ready, 1)
            dve.wait_ge(w23_in, 48)
            for kind, t, i in SCHEDULE:
                follow(kind, t, i)


def kernel(**inputs):
    import numpy as np
    import concourse.bacc as bacc
    from concourse.bass_utils import run_bass_kernel_spmd

    w_top1 = np.asarray(inputs["W_top1"])
    pairs = N * (N - 1) // 2
    w_pair = np.zeros((QUADS, NP_, PAIR_TILES, H1), w_top1.dtype)
    order = [0] + [1 + f for f in FIELD_AT[1:]]
    for m in range(1, N):
        s, jj = divmod(m - 1, QUADS)
        for n in range(m):
            a, b = sorted((order[n], order[m]))
            w_pair[jj, n, s] = w_top1[D + a * (2 * N - a - 1) // 2 + (b - a - 1)]
    arrays = {
        "x": np.asarray(inputs["r_dense_features"]),
        "ids": np.asarray(inputs["ids"]),
        "ids_by_field": np.asarray(inputs["ids"]).T,
        "w_pair": w_pair.reshape(P, PAIR_TILES, H1),
        "w_dense": np.stack([w_top1[0:D], w_top1[D + pairs:]]),
        "b1": np.asarray(inputs["b_top1"]).reshape(H1 // P, P).T,
        "w2": np.asarray(inputs["W_top2"]),
        "b2": np.asarray(inputs["b_top2"]).reshape(H2 // P, P).T,
        "w3": np.asarray(inputs["W_top3"]).reshape(H2 // P, P).T,
    }
    for f in range(FIELDS):
        arrays[f"tbl_{f}"] = np.asarray(inputs[f"tbl_{f}"])
    arrays = {f"in_{k}": np.ascontiguousarray(a) for k, a in arrays.items()}

    nc = bacc.Bacc("TRN2", target_bir_lowering=False, num_devices=1)
    ap = {k: nc.dram_tensor(k, a.shape, mybir.dt.from_np(a.dtype), kind="ExternalInput").ap()
          for k, a in arrays.items()}
    y = nc.dram_tensor("out_y", (BATCH, 1), F32, kind="ExternalOutput").ap()
    dlrm_tower(nc, ap["in_x"], ap["in_ids"], ap["in_ids_by_field"], [ap[f"in_tbl_{f}"] for f in range(FIELDS)], ap["in_w_pair"],
               ap["in_w_dense"], ap["in_b1"], ap["in_w2"], ap["in_b2"], ap["in_w3"],
               y.rearrange("b a -> a b"))
    r = run_bass_kernel_spmd(nc, [arrays], core_ids=[0])
    return r.results[0]["out_y"]
```

```python
from contextlib import ExitStack

import concourse.bass as bass
from concourse import mybir

ALU = mybir.AluOpType
ACT = mybir.ActivationFunctionType
F32 = mybir.dt.float32
F16 = mybir.dt.float16
F32R = mybir.dt.float32r
I32 = mybir.dt.int32

P = 128
BATCH = 512
D = 128
FIELDS = 26
N = FIELDS + 1
PADDED_N = 32
TILES = BATCH // P
QUADS = 4
GROUPS = P // QUADS
H1, H2 = 512, 256

TABLE_ROWS = [1000, 1000, 1000, 1250, 1250, 125000, 1000, 1000, 1000, 12500, 1000, 1250, 1250,
              12500, 12500, 1000, 12500, 12500, 12500, 12500, 1000, 1250, 12500, 1250, 1000, 1250]
CHUNKS = 8
PICKED_ROWS = 1000
K = 8
PICKED = [f for f in range(FIELDS) if TABLE_ROWS[f] == PICKED_ROWS][:K]
GATHERED = [f for f in range(FIELDS) if f not in PICKED]
ROWS_PER_CHUNK = PICKED_ROWS // CHUNKS
FIELD_AT = [None] + PICKED + GATHERED

SPARSE_TILES = -(-N // QUADS)
SHIFTS = N // 2 + 1
COMPACT_TILES = 3
N_PER = N // COMPACT_TILES
COMPACT_ROWS = N_PER * SHIFTS


def pair_at(n, k):
    if n + k < N:
        return n, n + k
    return (n + k - N, n + 1) if n + 1 < N and k < SHIFTS else None


assert sorted(filter(None, (pair_at(n, k) for n in range(N) for k in range(1, SHIFTS + 1)))) == \
    [(a, b) for a in range(N) for b in range(a + 1, N)]

VECTORS_PER_BANK = 4
BANKS_OF = [[0]] + [list(range(a, min(N, a + VECTORS_PER_BANK))) for a in range(K + 1, N, VECTORS_PER_BANK)]
BANKS = len(BANKS_OF)
GRAM_ROWS = (QUADS - 1) * PADDED_N + N
UNIT = 8
UNITS = GROUPS // UNIT
WARM_UP_ROUNDS = 5
CHUNKS_BY_ACT = 1
LO_AT = (1, 3)


def schedule():
    def banks(t, *numbers):
        return [("bank", t, q) for q in numbers]

    def grams(t, *units):
        return [("grams", t, u) for u in units]

    def layer1(t, *parts):
        return [("layer1", t, i) for i in parts]

    first, layer2, layer3 = ([[(kind, t, 0)] for t in range(TILES)] for kind in ("first", "layer2", "layer3"))
    steps = []
    for i in range(K):
        steps += [("pick", 0, i), ("bank", *divmod(i, BANKS))]
    steps += grams(0, 0) + banks(1, 2) + grams(0, 1) + banks(1, 3) + grams(0, 2) + banks(1, 4, 5) + grams(0, 3)
    steps += banks(2, 0) + grams(1, 0) + banks(2, 1) + grams(1, 1) + banks(2, 2) + grams(1, 2, 3) + banks(2, 3)
    steps += first[0] + layer1(0, 0, 1, 2) + banks(2, 4) + layer2[0] + banks(2, 5) + layer3[0] + banks(3, 0)
    steps += grams(2, 0, 1) + banks(3, 1) + grams(2, 2, 3)
    steps += first[1] + layer1(1, 0, 1, 2) + banks(3, 2) + layer2[1] + banks(3, 3) + layer3[1]
    steps += first[2] + layer1(2, 0) + banks(3, 4) + layer1(2, 1, 2) + banks(3, 5) + layer2[2]
    steps += grams(3, 0) + layer3[2] + grams(3, 1, 2, 3)
    steps += first[3] + layer1(3, 0, 1, 2, 3) + layer2[3] + layer3[3]
    return steps


SCHEDULE = schedule()
assert [(t, q) for kind, t, q in SCHEDULE if kind == "bank"] == [(t, q) for t in range(TILES) for q in range(BANKS)]
assert len(set(SCHEDULE)) == len(SCHEDULE)


def copies_by_act(t, q):
    return t == 0 or (BANKS * t + q) % 2 == 1


def copies_until(t, q, by_act):
    return sum(copies_by_act(*divmod(i, BANKS)) == by_act for i in range(BANKS * t + q + 1))


PARTS = [2 if o == 0 else 1 for o in range(K)]


def chunks_of(o, part):
    return slice(CHUNKS // PARTS[o] * part, CHUNKS // PARTS[o] * (part + 1))


def parts_until(o, part):
    return sum(PARTS[:o]) + part + 1


def slots_of(quad):
    return len(range(quad, N, QUADS))


def dlrm_tower(nc, x, ids, ids_by_field, tables, w_sparse, w_compact, w_twice, b1, w2, b2, w3, gram_dram, y):
    with ExitStack() as ctx:
        def sb(name, shape, dt=F32):
            return ctx.enter_context(nc.sbuf_tensor(name, shape, dt))

        def sem(name):
            return ctx.enter_context(nc.semaphore(name))

        idx = sb("idx", [P, TILES, FIELDS], I32)
        ids_bc = sb("ids_bc", [ROWS_PER_CHUNK, 2, BATCH], I32)
        ids_h = sb("ids_h", [ROWS_PER_CHUNK, 2, BATCH], F16)
        minus_row_int = sb("minus_row_int", [ROWS_PER_CHUNK, CHUNKS], I32)
        minus_row = sb("minus_row", [ROWS_PER_CHUNK, CHUNKS])
        distance = sb("distance", [ROWS_PER_CHUNK, BATCH])
        table = sb("table", [ROWS_PER_CHUNK, 2, CHUNKS, D])
        table_hi = sb("table_hi", [ROWS_PER_CHUNK, 2, CHUNKS, D], F32R)
        table_lo = sb("table_lo", [ROWS_PER_CHUNK, 2, CHUNKS, D], F32R)
        onehot = sb("onehot", [ROWS_PER_CHUNK, 2, CHUNKS, BATCH], F32R)
        x_sb = sb("x_sb", [P, TILES, D])
        emb = sb("emb", [P, 2, len(GATHERED), D])
        vT = sb("vT", [P, TILES, GROUPS, QUADS, PADDED_N])
        xT = sb("xT", [P, TILES, P])
        ident = sb("ident", [P, P])
        z_sparse = sb("z_sparse", [P, TILES, SPARSE_TILES, P])
        z_compact = sb("z_compact", [COMPACT_ROWS, TILES - 1, COMPACT_TILES, P])
        ws_sb = sb("ws_sb", [P, SPARSE_TILES, H1])
        wc_sb = sb("wc_sb", [COMPACT_ROWS, COMPACT_TILES, H1])
        wd2_sb = sb("wd2_sb", [P, 2, H1])
        wd_sb = sb("wd_sb", [P, H1])
        b1_sb = sb("b1_sb", [P, H1 // P])
        w2_sb = sb("w2_sb", [P, H1 // P, H2])
        b2_sb = sb("b2_sb", [P, H2 // P])
        w3_sb = sb("w3_sb", [P, H2 // P])
        h1T = sb("h1T", [P, H1 // P, P])
        h2T = sb("h2T", [P, H2 // P, P])
        y_sb = sb("y_sb", [1, BATCH])

        ps_t = [ctx.enter_context(nc.psum_tensor(f"ps_t{i}", [P, VECTORS_PER_BANK, P], F32)) for i in range(2)]
        ps_g = [ctx.enter_context(nc.psum_tensor(f"ps_g{i}", [P, UNIT, P], F32)) for i in range(2)]
        ps_act = ctx.enter_context(nc.psum_tensor("ps_act", [P, 4, P], F32))
        ps_dve = ctx.enter_context(nc.psum_tensor("ps_dve", [P, 4, P], F32))

        ids_in = sem("ids_in")
        x_in = sem("x_in")
        w1_in = sem("w1_in")
        w23_in = sem("w23_in")
        ws_in = sem("ws_in")
        ident_zero = sem("ident_zero")
        ident_ready = sem("ident_ready")
        pads_ready = sem("pads_ready")
        gathered = [[sem(f"gathered_{t}_{q}") for q in range(BANKS)] for t in range(TILES)]
        ids_bc_in = [sem(f"ids_bc_in{o}") for o in range(K)]
        table_in = [[sem(f"table_in{o}_{part}") for part in range(PARTS[o])] for o in range(K)]
        minus_row_int_ready = sem("minus_row_int_ready")
        ids_h_ready = sem("ids_h_ready")
        minus_row_ready = sem("minus_row_ready")
        onehot_dve = sem("onehot_dve")
        distance_ready = sem("distance_ready")
        onehot_act = sem("onehot_act")
        hi_ready = sem("hi_ready")
        lo_ready = sem("lo_ready")
        picked = sem("picked")
        picked_act = sem("picked_act")
        transposed = sem("transposed")
        vT_dve = sem("vT_dve")
        vT_act = sem("vT_act")
        gram_done = sem("gram_done")
        gram_dve = sem("gram_dve")
        gram_act = sem("gram_act")
        z_stored = [sem(f"z_stored{t}") for t in range(TILES - 1)]
        z_loaded = [[sem(f"z_loaded{t}_{i}") for i in range(COMPACT_TILES)] for t in range(TILES - 1)]
        wd_ready = sem("wd_ready")
        l1_for_act = sem("l1_for_act")
        l1_for_dve = sem("l1_for_dve")
        h1_dve = sem("h1_dve")
        h1_act = sem("h1_act")
        l2_for_act = sem("l2_for_act")
        l2_for_dve = sem("l2_for_dve")
        h2_dve = sem("h2_dve")
        h2_act = sem("h2_act")
        l3_done = sem("l3_done")
        y_ready = sem("y_ready")
        y_stored = sem("y_stored")

        ps_pick = [ps_g[i][:, 0:UNIT // 2, :] for i in range(2)]

        def first_layer_sum(t, c):
            if t == TILES - 1:
                return (ps_act, ps_t[0], ps_dve, ps_t[1])[c][:, 0, :]
            return (ps_act, ps_dve)[c // 2][:, c % 2, :]

        def table_rows(o):
            return tables[PICKED[o]].rearrange("(p c) d -> p c d", c=CHUNKS)

        def field_ids(o):
            return ids_by_field[PICKED[o]:PICKED[o] + 1, :].broadcast_to([ROWS_PER_CHUNK, BATCH])

        block = ctx.enter_context(nc.Block())

        @block.sync
        def _(sp):
            sp.dma_start(idx[:], ids.rearrange("(t p) f -> p t f", p=P)).then_inc(ids_in, 16)

            def load_table(o):
                if o >= 2:
                    sp.wait_ge(ids_h_ready, o - 1)
                if o > 0:
                    sp.dma_start(ids_bc[:, o % 2, :], field_ids(o)).then_inc(ids_bc_in[o], 16)
                if o >= 2:
                    sp.wait_ge(lo_ready, parts_until(o - 2, PARTS[o - 2] - 1))
                for part in range(PARTS[o]):
                    cs = chunks_of(o, part)
                    sp.dma_start(table[:, o % 2, cs, :], table_rows(o)[:, cs, :]).then_inc(table_in[o][part], 16)

            load_table(0)
            load_table(1)
            sp.dma_start(x_sb[:], x.rearrange("(t p) d -> p t d", p=P)).then_inc(x_in, 16)
            for o in range(2, K):
                load_table(o)
            sp.dma_start(wd2_sb[:], w_twice.rearrange("a r o -> r a o")).then_inc(w1_in, 16)
            sp.dma_start(b1_sb[:], b1).then_inc(w1_in, 16)
            sp.dma_start(wc_sb[:], w_compact).then_inc(w1_in, 16)
            sp.dma_start(w2_sb[:], w2.rearrange("(c r) o -> r c o", r=P)).then_inc(w23_in, 16)
            sp.dma_start(b2_sb[:], b2).then_inc(w23_in, 16)
            sp.dma_start(w3_sb[:], w3).then_inc(w23_in, 16)
            sp.dma_start(ws_sb[:], w_sparse).then_inc(ws_in, 16)
            for t in range(TILES - 1):
                sp.wait_ge(gram_dve, UNITS * (t + 1))
                sp.wait_ge(gram_act, UNITS * (t + 1))
                for jj in range(QUADS):
                    rows = slice(PADDED_N * jj, PADDED_N * jj + N + 1)
                    sp.dma_start(gram_dram[t, :, jj:N:QUADS, :],
                                 z_sparse[rows, t, 0:slots_of(jj), :]).then_inc(z_stored[t], 16)
                sp.wait_ge(z_stored[t], 16 * QUADS)
                for i in range(COMPACT_TILES):
                    n0 = i * N_PER
                    entries = bass.AP(tensor=gram_dram.tensor, offset=((t * (N + 1) + n0) * N + n0 + 1) * P,
                                      ap=[[(N + 1) * P, N_PER], [P, SHIFTS], [1, P]])
                    sp.dma_start(z_compact[:, t, i, :], entries).then_inc(z_loaded[t][i], 16)
            sp.wait_ge(y_ready, TILES)
            sp.dma_start(y, y_sb[:]).then_inc(y_stored, 16)
            sp.wait_ge(y_stored, 16)

        @block.gpsimd
        def _(pool):
            nc.gpsimd.iota(minus_row_int[:], pattern=[[-1, CHUNKS]], base=0, channel_multiplier=-CHUNKS)\
                .then_inc(minus_row_int_ready, 1)
            nc.gpsimd.memset(ident[:], 0.0).then_inc(ident_zero, 1)
            pool.wait_ge(ident_zero, 1)
            nc.gpsimd.affine_select(out=ident[:], in_=ident[:], compare_op=ALU.not_equal, fill=1.0, base=0,
                                    pattern=[[-1, P]], channel_multiplier=1).then_inc(ident_ready, 1)
            for t in range(TILES):
                if t == 0:
                    pool.wait_ge(ids_in, 16)
                for q in range(1, BANKS):
                    if t >= 2:
                        pool.wait_ge(transposed, BANKS * (t - 2) + q + 1)
                    for n in BANKS_OF[q]:
                        f = FIELD_AT[n]
                        nc.gpsimd.indirect_dma_start(
                            out=emb[:, t % 2, n - K - 1, :], out_offset=None, in_=tables[f],
                            in_offset=bass.IndirectOffsetOnAxis(ap=idx[:, t, f:f + 1], axis=0)
                        ).then_inc(gathered[t][q], 16)

        @block.tensor
        def _(pe):
            def pick(o):
                if o >= 2:
                    pe.wait_ge(picked_act, o - 1)
                for c in range(CHUNKS):
                    for part in range(PARTS[o]):
                        if c == chunks_of(o, part).start:
                            pe.wait_ge(lo_ready, parts_until(o, part))
                    by_act = c - (CHUNKS - CHUNKS_BY_ACT)
                    if by_act < 0:
                        pe.wait_ge(onehot_dve, (CHUNKS - CHUNKS_BY_ACT) * o + c + 1)
                    else:
                        pe.wait_ge(onehot_act, CHUNKS_BY_ACT * o + by_act + 1)
                    nc.tensor.matmul(ps_pick[o % 2], table_hi[:, o % 2, c, :], onehot[:, o % 2, c, :],
                                     start=(c == 0), stop=False)
                    nc.tensor.matmul(ps_pick[o % 2], table_lo[:, o % 2, c, :], onehot[:, o % 2, c, :],
                                     start=False, stop=(c == CHUNKS - 1)).then_inc(picked, 1)

            def transpose_bank(t, q):
                i = BANKS * t + q
                if i >= 2:
                    t2, q2 = divmod(i - 2, BANKS)
                    by_act = copies_by_act(t2, q2)
                    pe.wait_ge(vT_act if by_act else vT_dve, copies_until(t2, q2, by_act))
                if i == 0:
                    pe.wait_ge(x_in, 16)
                if q > 0:
                    pe.wait_ge(gathered[t][q], 16 * len(BANKS_OF[q]))
                for s, n in enumerate(BANKS_OF[q]):
                    src = x_sb[:, t, :] if n == 0 else emb[:, t % 2, n - K - 1, :]
                    last = nc.tensor.transpose(ps_t[i % 2][:, s, :], src, ident[:])
                last.then_inc(transposed, 1)

            def grams(t, u):
                if t == 0 and u == 0:
                    pe.wait_ge(pads_ready, 3)
                    pe.wait_ge(picked_act, K)
                if u == 0:
                    for by_act in (False, True):
                        n = copies_until(t, BANKS - 1, by_act)
                        if n:
                            pe.wait_ge(vT_act if by_act else vT_dve, n)
                k = UNITS * t + u
                if k >= 2:
                    pe.wait_ge(gram_dve, k - 1)
                    pe.wait_ge(gram_act, k - 1)
                for g in range(UNIT):
                    v = vT[:, t, u * UNIT + g, :, :]
                    out = ps_g[k % 2][0:GRAM_ROWS, g, 0:QUADS * N].rearrange("p (j m) -> p j m", j=QUADS)
                    last = nc.tensor.matmul(out, v.rearrange("p j n -> p (j n)")[:, 0:GRAM_ROWS], v[:, :, 0:N],
                                            start=True, stop=True)
                last.then_inc(gram_done, 1)

            def first(t):
                if t == 0:
                    pe.wait_ge(w1_in, 48)
                    pe.wait_ge(wd_ready, 1)
                for c in (2, 3, 0, 1):
                    if c == 2 and t >= 1:
                        pe.wait_ge(h2_dve, t)
                    if c == 0 and t >= 1:
                        pe.wait_ge(y_ready, t)
                    nc.tensor.matmul(first_layer_sum(t, c), wd_sb[:, c * P:(c + 1) * P], xT[:, t, :],
                                     start=(c % 2 == 0 or t == TILES - 1), stop=False, skip_group_check=True)

            def layer1(t, i):
                if t < TILES - 1:
                    pe.wait_ge(z_loaded[t][i], 16)
                    products = [(c, wc_sb[:, i, :], z_compact[:, t, i, :], i == COMPACT_TILES - 1)
                                for c in range(H1 // P)]
                else:
                    if i == 0:
                        pe.wait_ge(ws_in, 16)
                        pe.wait_ge(gram_dve, UNITS * (t + 1))
                        pe.wait_ge(gram_act, UNITS * (t + 1))
                    products = [(i, ws_sb[:, s, :], z_sparse[:, t, s, :], s == SPARSE_TILES - 1)
                                for s in range(SPARSE_TILES)]
                for c, w, z, closes in products:
                    product = nc.tensor.matmul(first_layer_sum(t, c), w[:, c * P:(c + 1) * P], z,
                                               start=False, stop=closes, skip_group_check=True)
                    if closes:
                        product.then_inc((l1_for_act, l1_for_dve)[c // 2], 1)

            def layer2(t):
                if t == 0:
                    pe.wait_ge(w23_in, 48)
                chunks = [(c, k) for c in range(H2 // P) for k in range(H1 // P)]
                if t == TILES - 1:
                    chunks.sort(key=lambda ck: ck[1] == H1 // P - 1)
                for c, k in chunks:
                    if c == 0:
                        pe.wait_ge((h1_act, h1_dve)[k // 2], 2 * t + (k % 2 + 1 if t == TILES - 1 else 2))
                    last = nc.tensor.matmul((ps_act, ps_dve)[c][:, 2, :], w2_sb[:, k, c * P:(c + 1) * P],
                                            h1T[:, k, :], start=(k == 0), stop=(k == H1 // P - 1))
                    if k == H1 // P - 1:
                        last.then_inc((l2_for_act, l2_for_dve)[c], 1)

            def layer3(t):
                pe.wait_ge(h2_act, t + 1)
                for k in range(H2 // P):
                    if k == 1:
                        pe.wait_ge(h2_dve, t + 1)
                    last = nc.tensor.matmul(ps_act[0:1, 3, :], w3_sb[:, k:k + 1], h2T[:, k, :],
                                            start=(k == 0), stop=(k == H2 // P - 1))
                last.then_inc(l3_done, 1)

            pe.wait_ge(ident_ready, 1)
            with pe.Fori(0, WARM_UP_ROUNDS):
                for _ in range(2):
                    nc.tensor.matmul(ps_pick[1][:, 0, :], ident[:], ident[:], start=True, stop=True)
            for kind, t, i in SCHEDULE:
                if kind == "pick":
                    pick(i)
                elif kind == "bank":
                    transpose_bank(t, i)
                elif kind == "grams":
                    grams(t, i)
                elif kind == "first":
                    first(t)
                elif kind == "layer1":
                    layer1(t, i)
                elif kind == "layer2":
                    layer2(t)
                elif kind == "layer3":
                    layer3(t)

        def copy_transposes(eng, copy, ready, t, q):
            i = BANKS * t + q
            eng.wait_ge(transposed, i + 1)
            fs = BANKS_OF[q]
            src = ps_t[i % 2][:, 0:len(fs), :].rearrange("p f (j g) -> p f j g", j=QUADS)
            dst = vT[:, t, :, :, fs[0]:fs[-1] + 1].rearrange("p g j f -> p f j g")
            if q == 0:
                copy(xT[:, t, :], ps_t[i % 2][:, 0, :])
            copy(dst, src).then_inc(ready, 1)

        def copy_grams(eng, copy, ready, quads, t, u):
            k = UNITS * t + u
            eng.wait_ge(gram_done, k + 1)
            for j in quads:
                rows = min(PADDED_N, GRAM_ROWS - PADDED_N * j)
                for jj in range(QUADS):
                    ns = slots_of(jj)
                    c0 = j * N + jj
                    src = ps_g[k % 2][PADDED_N * j:PADDED_N * j + rows, :, c0:c0 + QUADS * (ns - 1) + 1:QUADS]
                    b0 = GROUPS * j + u * UNIT
                    last = copy(z_sparse[PADDED_N * jj:PADDED_N * jj + rows, t, 0:ns, b0:b0 + UNIT],
                                src.rearrange("p g s -> p s g"))
            last.then_inc(ready, 1)

        def chunks_at(kind, t, i, c0):
            if kind != "layer1":
                return []
            if t == TILES - 1:
                return [(i, 2 * t + i - c0 + 1)] if i in (c0, c0 + 1) else []
            return [(c0, 2 * t + 2), (c0 + 1, 2 * t + 2)] if i == COMPACT_TILES - 1 else []

        @block.scalar
        def _(act):
            def copy(dst, src):
                return nc.scalar.activation(dst, src, ACT.Copy)

            def follow(kind, t, i):
                if kind == "pick":
                    if i + 2 < K:
                        convert_ids(i + 2)
                    act.wait_ge(picked, CHUNKS * (i + 1))
                    if i + 2 < K:
                        split_hi(i + 2, 0)
                    src = ps_pick[i % 2].rearrange("p t (j g) -> p t j g", j=QUADS)
                    copy(vT[:, :, :, :, 1 + i].rearrange("p t g j -> p t j g"), src).then_inc(picked_act, 1)
                    if i + 2 < K:
                        make_onehot(i + 2)
                if kind == "bank" and copies_by_act(t, i):
                    copy_transposes(act, copy, vT_act, t, i)
                if kind == "grams":
                    copy_grams(act, copy, gram_act, (2, 3), t, i)
                if (kind, t, i) == ("layer1", 0, 0):
                    act.wait_ge(w1_in, 48)
                    act.wait_ge(w23_in, 48)
                for c, sums in chunks_at(kind, t, i, 0):
                    act.wait_ge(l1_for_act, sums)
                    if t >= 1:
                        act.wait_ge(l2_for_dve, t)
                    nc.scalar.activation(h1T[:, c, :], first_layer_sum(t, c), ACT.Relu, bias=b1_sb[:, c:c + 1])\
                        .then_inc(h1_act, 1)
                if kind == "layer2":
                    act.wait_ge(l2_for_act, t + 1)
                    nc.scalar.activation(h2T[:, 0, :], ps_act[:, 2, :], ACT.Relu, bias=b2_sb[:, 0:1])\
                        .then_inc(h2_act, 1)
                if kind == "layer3":
                    act.wait_ge(l3_done, t + 1)
                    nc.scalar.activation(y_sb[0:1, t * P:(t + 1) * P], ps_act[0:1, 3, :], ACT.Copy)\
                        .then_inc(y_ready, 1)

            act.dma_start(ids_bc[:, 0, :], field_ids(0)).then_inc(ids_bc_in[0], 16)

            def make_onehot(o):
                act.wait_ge(ids_h_ready, o + 1)
                if o == 0:
                    act.wait_ge(minus_row_ready, 1)
                for i in range(CHUNKS_BY_ACT):
                    c = CHUNKS - CHUNKS_BY_ACT + i
                    done = CHUNKS_BY_ACT * o + i
                    if o >= 2:
                        act.wait_ge(picked, CHUNKS * (o - 2) + c + 1)
                    if done > 0:
                        act.wait_ge(onehot_act, done)
                    nc.scalar.activation(distance[:], ids_h[:, o % 2, :], ACT.Abs, bias=minus_row[:, c:c + 1])\
                        .then_inc(distance_ready, 1)
                    act.wait_ge(distance_ready, done + 1)
                    nc.scalar.activation(onehot[:, o % 2, c, :], distance[:], ACT.Relu, bias=1.0, scale=-1.0)\
                        .then_inc(onehot_act, 1)

            def convert_ids(o):
                act.wait_ge(ids_bc_in[o], 16)
                if o >= 2:
                    act.wait_ge(onehot_dve, (CHUNKS - CHUNKS_BY_ACT) * (o - 1))
                    act.wait_ge(distance_ready, CHUNKS_BY_ACT * (o - 1))
                copy(ids_h[:, o % 2, :], ids_bc[:, o % 2, :]).then_inc(ids_h_ready, 1)

            def split_hi(o, part):
                act.wait_ge(table_in[o][part], 16)
                if o >= 2:
                    act.wait_ge(picked, CHUNKS * (o - 1))
                cs = chunks_of(o, part)
                copy(table_hi[:, o % 2, cs], table[:, o % 2, cs]).then_inc(hi_ready, 1)

            convert_ids(0)
            split_hi(0, 0)
            split_hi(0, 1)
            convert_ids(1)
            make_onehot(0)
            split_hi(1, 0)
            make_onehot(1)
            for kind, t, i in SCHEDULE:
                follow(kind, t, i)

        @block.vector
        def _(dve):
            def copy(dst, src):
                return nc.vector.tensor_copy(dst, src)

            def follow(kind, t, i):
                if kind == "bank" and not copies_by_act(t, i):
                    copy_transposes(dve, copy, vT_dve, t, i)
                if kind == "grams":
                    copy_grams(dve, copy, gram_dve, (0, 1), t, i)
                if (kind, t, i) == ("grams", 0, UNITS - 1):
                    dve.wait_ge(w1_in, 48)
                    nc.vector.tensor_tensor(wd_sb[:], wd2_sb[:, 0, :], wd2_sb[:, 1, :], ALU.add).then_inc(wd_ready, 1)
                if (kind, t, i) == ("layer1", 0, 0):
                    dve.wait_ge(w23_in, 48)
                for c, sums in chunks_at(kind, t, i, 2):
                    dve.wait_ge(l1_for_dve, sums)
                    if t >= 1:
                        dve.wait_ge(l2_for_dve, t)
                    nc.vector.tensor_scalar(h1T[:, c, :], first_layer_sum(t, c), b1_sb[:, c:c + 1], 0.0,
                                            ALU.add, ALU.max).then_inc(h1_dve, 1)
                if kind == "layer2":
                    dve.wait_ge(l2_for_dve, t + 1)
                    if t >= 1:
                        dve.wait_ge(l3_done, t)
                    nc.vector.tensor_scalar(h2T[:, 1, :], ps_dve[:, 2, :], b2_sb[:, 1:2], 0.0, ALU.add, ALU.max)\
                        .then_inc(h2_dve, 1)

            nc.vector.memset(vT[:, :, :, :, N:PADDED_N], 0.0).then_inc(pads_ready, 1)
            dve.wait_ge(minus_row_int_ready, 1)
            nc.vector.tensor_copy(minus_row[:], minus_row_int[:]).then_inc(minus_row_ready, 1)
            dve.wait_ge(minus_row_ready, 1)

            def split_lo(o, part):
                dve.wait_ge(table_in[o][part], 16)
                dve.wait_ge(hi_ready, parts_until(o, part))
                if o >= 2:
                    dve.wait_ge(picked, CHUNKS * (o - 1))
                cs = chunks_of(o, part)
                nc.vector.tensor_tensor(table_lo[:, o % 2, cs], table[:, o % 2, cs],
                                        table_hi[:, o % 2, cs].bitcast(F32), ALU.subtract).then_inc(lo_ready, 1)

            for o in range(K):
                if o > 0:
                    split_lo(o, 0)
                dve.wait_ge(ids_h_ready, o + 1)
                for c in range(CHUNKS - CHUNKS_BY_ACT):
                    if o == 0 and c in LO_AT:
                        split_lo(0, LO_AT.index(c))
                    if o >= 2:
                        dve.wait_ge(picked, CHUNKS * (o - 2) + c + 1)
                    nc.vector.tensor_scalar(onehot[:, o % 2, c, :], ids_h[:, o % 2, :], minus_row[:, c:c + 1], 0.0,
                                            ALU.add, ALU.is_equal).then_inc(onehot_dve, 1)
            nc.vector.memset(z_sparse[:, :, :, (QUADS - 1) * GROUPS:P], 0.0).then_inc(pads_ready, 1)
            no_m = slice(PADDED_N * (QUADS - 1), P)
            nc.vector.memset(z_sparse[no_m, TILES - 1, SPARSE_TILES - 1, 0:(QUADS - 1) * GROUPS], 0.0)\
                .then_inc(pads_ready, 1)
            for kind, t, i in SCHEDULE:
                follow(kind, t, i)


def kernel(**inputs):
    import numpy as np
    import concourse.bacc as bacc
    from concourse.bass_utils import run_bass_kernel_spmd

    w_top1 = np.asarray(inputs["W_top1"])
    pairs = N * (N - 1) // 2
    order = [0] + [1 + f for f in FIELD_AT[1:]]

    def weights_of(lower, upper):
        a, b = sorted((order[lower], order[upper]))
        return w_top1[D + a * (2 * N - a - 1) // 2 + (b - a - 1)]

    w_sparse = np.zeros((QUADS, PADDED_N, SPARSE_TILES, H1), w_top1.dtype)
    for m in range(1, N):
        s, jj = divmod(m, QUADS)
        for n in range(m):
            w_sparse[jj, n, s] = weights_of(n, m)
    w_compact = np.zeros((N_PER, SHIFTS, COMPACT_TILES, H1), w_top1.dtype)
    for n in range(N):
        for k in range(1, SHIFTS + 1):
            if pair_at(n, k):
                w_compact[n % N_PER, k - 1, n // N_PER] = weights_of(*pair_at(n, k))
    arrays = {
        "x": np.asarray(inputs["r_dense_features"]),
        "ids": np.asarray(inputs["ids"]),
        "ids_by_field": np.asarray(inputs["ids"]).T,
        "w_sparse": w_sparse.reshape(P, SPARSE_TILES, H1),
        "w_compact": w_compact.reshape(COMPACT_ROWS, COMPACT_TILES, H1),
        "w_twice": np.stack([w_top1[0:D], w_top1[D + pairs:]]),
        "b1": np.asarray(inputs["b_top1"]).reshape(H1 // P, P).T,
        "w2": np.asarray(inputs["W_top2"]),
        "b2": np.asarray(inputs["b_top2"]).reshape(H2 // P, P).T,
        "w3": np.asarray(inputs["W_top3"]).reshape(H2 // P, P).T,
    }
    for f in range(FIELDS):
        arrays[f"tbl_{f}"] = np.asarray(inputs[f"tbl_{f}"])
    arrays = {f"in_{k}": np.ascontiguousarray(a) for k, a in arrays.items()}

    nc = bacc.Bacc("TRN2", target_bir_lowering=False, num_devices=1)
    ap = {k: nc.dram_tensor(k, a.shape, mybir.dt.from_np(a.dtype), kind="ExternalInput").ap()
          for k, a in arrays.items()}
    gram_dram = nc.dram_tensor("gram_dram", (TILES - 1, N + 1, N, P), F32, kind="Internal").ap()
    y = nc.dram_tensor("out_y", (BATCH, 1), F32, kind="ExternalOutput").ap()
    dlrm_tower(nc, ap["in_x"], ap["in_ids"], ap["in_ids_by_field"], [ap[f"in_tbl_{f}"] for f in range(FIELDS)],
               ap["in_w_sparse"], ap["in_w_compact"], ap["in_w_twice"], ap["in_b1"], ap["in_w2"], ap["in_b2"],
               ap["in_w3"], gram_dram, y.rearrange("b a -> a b"))
    r = run_bass_kernel_spmd(nc, [arrays], core_ids=[0])
    return r.results[0]["out_y"]
```
